# Optimizing a Trainium2 kernel written in Bass

```python
import numpy as np
import jax
import jax.numpy as jnp

def _softmax(x, axis=-1):
    return jax.nn.softmax(x, axis=axis)

def _gelu(x):
    return jax.nn.gelu(x, approximate=True)

def _silu(x):
    return jax.nn.silu(x)

def _sigmoid(x):
    return jax.nn.sigmoid(x)

def _layernorm(x, axis=-1, eps=1e-05):
    m = jnp.mean(x, axis=axis, keepdims=True)
    v = jnp.var(x, axis=axis, keepdims=True)
    return (x - m) / jnp.sqrt(v + eps)

def _scatter_add(tgt, idx, src, axis=0):
    return tgt.at[idx].add(src)

def _segment_sum(src, seg, n):
    return jax.ops.segment_sum(src, seg, n)
kernel_name = 'mk_gnn_preln_d4_gnn_r8_4585ca'

def setup_inputs(seed: int=0):
    np.random.seed(seed)
    _w = jnp.asarray

    def _rec_inputs():
        import jax
        import jax.numpy as jnp
        _gk = jax.random.key(seed)
        x = -0.000202 + 1 * jax.random.normal(jax.random.fold_in(_gk, 1), (12500, 64), jnp.float32)
        _s = jax.random.randint(jax.random.fold_in(_gk, 2), (100000,), 0, 12500, jnp.int32)
        _d = jax.random.randint(jax.random.fold_in(_gk, 3), (100000,), 0, 12500, jnp.int32)
        _loop = jnp.arange(12500, dtype=jnp.int32)
        src = jnp.concatenate([_s, _d, _loop])
        dst = jnp.concatenate([_d, _s, _loop])
        _o = jnp.argsort(dst, stable=True)
        src = src[_o]
        dst = dst[_o]
        edge_attr_64 = -8.16379e-05 + 0.999858 * jax.random.normal(jax.random.fold_in(_gk, 12), (212500, 64), jnp.float32)
        return (x, src, dst, edge_attr_64)
    x, src, dst, edge_attr_64 = _rec_inputs()

    def _L0_gnn_setup():
        import jax, jax.numpy as jnp
        import numpy as np
        N_NODES = 12500
        N_EDGES = 200000
        D_FEAT = 64
        key = jax.random.key(seed)
        k1, k2, k3, k4 = jax.random.split(key, 4)
        features = jax.random.normal(k1, (N_NODES, D_FEAT), dtype=jnp.float32)
        W = jax.random.uniform(k2, (D_FEAT,), dtype=jnp.float32)
        src = jax.random.randint(k3, (N_EDGES,), 0, N_NODES, dtype=jnp.int32)
        dst = jax.random.randint(k4, (N_EDGES,), 0, N_NODES, dtype=jnp.int32)
        return {'features': features, 'W': W, 'src': src, 'dst': dst}
    _L0_gnn_all = _L0_gnn_setup()
    _L0_gnn_in = {k: v for k, v in _L0_gnn_all.items() if k in ('W',)}
    del _L0_gnn_all

    def _L1_gnn_setup():
        import jax, jax.numpy as jnp
        import numpy as np
        N_NODES = 12500
        N_EDGES = 200000
        IN_C, HID_C, OUT_C = (64, 128, 64)

        def _glorot(key, shape):
            fan_in, fan_out = (shape[1], shape[0])
            s = jnp.sqrt(6.0 / (fan_in + fan_out))
            return jax.random.uniform(key, shape, jnp.float32, -s, s)

        def _sage_conv(x, src, dst, W_l, b, W_r, n_nodes):
            msg = x[src]
            agg = jax.ops.segment_sum(msg, dst, num_segments=n_nodes)
            cnt = jax.ops.segment_sum(jnp.ones((src.shape[0],), x.dtype), dst, num_segments=n_nodes)
            agg = agg / jnp.maximum(cnt, 1.0)[:, None]
            return agg @ W_l.T + b + x @ W_r.T
        key = jax.random.key(seed)
        ks = jax.random.split(key, 8)
        x = jax.random.normal(ks[0], (N_NODES, IN_C), jnp.float32)
        edge_index = jax.random.randint(ks[1], (2, N_EDGES), 0, N_NODES, jnp.int64)
        return {'x': x, 'edge_index': edge_index, 'W1_l': _glorot(ks[2], (HID_C, IN_C)), 'b1': jnp.zeros((HID_C,), jnp.float32), 'W1_r': _glorot(ks[3], (HID_C, IN_C)), 'W2_l': _glorot(ks[4], (OUT_C, HID_C)), 'b2': jnp.zeros((OUT_C,), jnp.float32), 'W2_r': _glorot(ks[5], (OUT_C, HID_C))}
    _L1_gnn_all = _L1_gnn_setup()
    _L1_gnn_in = {k: v for k, v in _L1_gnn_all.items() if k in ('W1_l', 'b1', 'W1_r', 'W2_l', 'b2', 'W2_r')}
    del _L1_gnn_all

    def _L2_gnn_setup():
        import jax, jax.numpy as jnp
        import numpy as np
        N_NODES = 12500

        def _segment_softmax(e, dst, num_segments):
            m = jax.ops.segment_max(e, dst, num_segments=num_segments)
            m = jnp.where(jnp.isfinite(m), m, 0.0)
            ex = jnp.exp(e - m[dst])
            denom = jax.ops.segment_sum(ex, dst, num_segments=num_segments)
            return ex / denom[dst]
        key = jax.random.key(seed)
        ks = jax.random.split(key, 8)
        N, E, Din, Dout = (N_NODES, 200000, 64, 64)
        node_h = jax.random.normal(ks[0], (N, Din), jnp.float32)
        edge_h = jax.random.normal(ks[1], (E, Din), jnp.float32)
        src = jax.random.randint(ks[2], (E,), 0, N, dtype=jnp.int32)
        dst = jax.random.randint(ks[3], (E,), 0, N, dtype=jnp.int32)
        s = float(np.sqrt(2.0 / (Din + Dout)))
        W_fc = jax.random.normal(ks[4], (Dout, Din), jnp.float32) * s
        W_fcr = jax.random.normal(ks[5], (Dout, Din), jnp.float32) * s
        loop_W = jax.random.normal(ks[6], (Dout, Dout), jnp.float32) * s
        return {'node_h': node_h, 'edge_h': edge_h, 'src': src, 'dst': dst, 'W_fc': W_fc, 'W_fcr': W_fcr, 'loop_W': loop_W}
    _L2_gnn_all = _L2_gnn_setup()
    _L2_gnn_in = {k: v for k, v in _L2_gnn_all.items() if k in ('W_fc', 'W_fcr', 'loop_W')}
    del _L2_gnn_all

    def _L3_gnn_setup():
        import jax, jax.numpy as jnp
        import numpy as np
        N = 12500
        E = 125000
        IN_DIM = 64
        OUT_DIM = 64
        key = jax.random.key(seed)
        k1, k2, k3, k4 = jax.random.split(key, 4)
        x = jax.random.normal(k1, (N, IN_DIM), dtype=jnp.float32)
        edge_index = jax.random.randint(k2, (2, E), 0, N, dtype=jnp.int64)
        bound = 1.0 / np.sqrt(IN_DIM)
        W = jax.random.uniform(k3, (OUT_DIM, IN_DIM), dtype=jnp.float32, minval=-bound, maxval=bound)
        b = jax.random.uniform(k4, (OUT_DIM,), dtype=jnp.float32, minval=-bound, maxval=bound)
        return {'x': x, 'edge_index': edge_index, 'W': W, 'b': b}
    _L3_gnn_all = _L3_gnn_setup()
    _L3_gnn_in = {k: v for k, v in _L3_gnn_all.items() if k in ('W', 'b')}
    del _L3_gnn_all
    return {'x': x, 'src': src, 'dst': dst, 'edge_attr_64': edge_attr_64, 'L0_gnn_W': _L0_gnn_in['W'], 'L1_gnn_W1_l': _L1_gnn_in['W1_l'], 'L1_gnn_b1': _L1_gnn_in['b1'], 'L1_gnn_W1_r': _L1_gnn_in['W1_r'], 'L1_gnn_W2_l': _L1_gnn_in['W2_l'], 'L1_gnn_b2': _L1_gnn_in['b2'], 'L1_gnn_W2_r': _L1_gnn_in['W2_r'], 'L2_gnn_W_fc': _L2_gnn_in['W_fc'], 'L2_gnn_W_fcr': _L2_gnn_in['W_fcr'], 'L2_gnn_loop_W': _L2_gnn_in['loop_W'], 'L3_gnn_W': _L3_gnn_in['W'], 'L3_gnn_b': _L3_gnn_in['b']}

def reference(x, src, dst, edge_attr_64, L0_gnn_W, L1_gnn_W1_l, L1_gnn_b1, L1_gnn_W1_r, L1_gnn_W2_l, L1_gnn_b2, L1_gnn_W2_r, L2_gnn_W_fc, L2_gnn_W_fcr, L2_gnn_loop_W, L3_gnn_W, L3_gnn_b):
    import jax
    import jax.numpy as jnp

    def _L0_gnn_ref(features, W, src, dst):
        import jax, jax.numpy as jnp
        import numpy as np
        N_NODES = 12500
        N_EDGES = 200000
        D_FEAT = 64
        h = features * W
        msgs = jnp.take(h, src, axis=0)
        out = jax.ops.segment_sum(msgs, dst, num_segments=N_NODES)
        return out

    def _L1_gnn_ref(x, edge_index, W1_l, b1, W1_r, W2_l, b2, W2_r):
        import jax, jax.numpy as jnp
        import numpy as np
        N_NODES = 12500
        N_EDGES = 200000
        IN_C, HID_C, OUT_C = (64, 128, 64)

        def _glorot(key, shape):
            fan_in, fan_out = (shape[1], shape[0])
            s = jnp.sqrt(6.0 / (fan_in + fan_out))
            return jax.random.uniform(key, shape, jnp.float32, -s, s)

        def _sage_conv(x, src, dst, W_l, b, W_r, n_nodes):
            msg = x[src]
            agg = jax.ops.segment_sum(msg, dst, num_segments=n_nodes)
            cnt = jax.ops.segment_sum(jnp.ones((src.shape[0],), x.dtype), dst, num_segments=n_nodes)
            agg = agg / jnp.maximum(cnt, 1.0)[:, None]
            return agg @ W_l.T + b + x @ W_r.T
        src, dst = (edge_index[0], edge_index[1])
        n = x.shape[0]
        h = _sage_conv(x, src, dst, W1_l, b1, W1_r, n)
        h = jax.nn.relu(h)
        out = _sage_conv(h, src, dst, W2_l, b2, W2_r, n)
        return jnp.squeeze(out)

    def _L2_gnn_ref(node_h, edge_h, src, dst, W_fc, W_fcr, loop_W):
        import jax, jax.numpy as jnp
        import numpy as np
        N_NODES = 12500

        def _segment_softmax(e, dst, num_segments):
            m = jax.ops.segment_max(e, dst, num_segments=num_segments)
            m = jnp.where(jnp.isfinite(m), m, 0.0)
            ex = jnp.exp(e - m[dst])
            denom = jax.ops.segment_sum(ex, dst, num_segments=num_segments)
            return ex / denom[dst]
        N = node_h.shape[0]
        h = node_h @ W_fc.T
        eh = edge_h @ W_fcr.T
        alpha = _segment_softmax(eh, dst, N)
        z = h[src]
        agg = jax.ops.segment_sum(alpha * (z + eh), dst, num_segments=N)
        deg = jax.ops.segment_sum(jnp.ones((dst.shape[0],), h.dtype), dst, num_segments=N)
        h_new = jnp.where((deg > 0)[:, None], agg + h @ loop_W, h)
        return jax.nn.relu(h_new)

    def _L3_gnn_ref(x, edge_index, W, b):
        import jax, jax.numpy as jnp
        import numpy as np
        N = 12500
        E = 125000
        IN_DIM = 64
        OUT_DIM = 64
        i = edge_index[0]
        j = edge_index[1]
        msg = x[j] @ W.T + b
        n = x.shape[0]
        out = jax.ops.segment_sum(msg, i, num_segments=n)
        deg = jax.ops.segment_sum(jnp.ones((i.shape[0],), dtype=msg.dtype), i, num_segments=n)
        deg = jnp.maximum(deg, 1.0)[:, None]
        return out / deg
    edge_index = jnp.stack([src, dst])
    h = jnp.maximum(_layernorm(x, axis=-1), 0.0)
    x = x + _L0_gnn_ref(h, L0_gnn_W, src, dst)
    h = jnp.maximum(_layernorm(x, axis=-1), 0.0)
    x = x + _L1_gnn_ref(h, edge_index, L1_gnn_W1_l, L1_gnn_b1, L1_gnn_W1_r, L1_gnn_W2_l, L1_gnn_b2, L1_gnn_W2_r)
    h = jnp.maximum(_layernorm(x, axis=-1), 0.0)
    x = x + _L2_gnn_ref(h, edge_attr_64, src, dst, L2_gnn_W_fc, L2_gnn_W_fcr, L2_gnn_loop_W)
    h = jnp.maximum(_layernorm(x, axis=-1), 0.0)
    x = x + _L3_gnn_ref(h, edge_index, L3_gnn_W, L3_gnn_b)
    return x

_drawn_inputs = setup_inputs


def setup_inputs(seed=0):
    import zlib

    import numpy as np

    out = dict(_drawn_inputs(seed))
    spreads = {'L1_gnn_b1': (0.0, 0.373), 'L1_gnn_b2': (0.0, 0.322)}
    factors = {'L3_gnn_b': 3.337}
    for name, (base, spread) in spreads.items():
        noise = np.random.default_rng([zlib.crc32(name.encode()), seed]).standard_normal(out[name].shape)
        drawn = base * np.exp(spread * noise) if base else spread * noise
        out[name] = jnp.asarray(drawn.astype(out[name].dtype))
    for name, factor in factors.items():
        out[name] = (out[name] * factor).astype(out[name].dtype)
    return out
```

```python
import numpy as np
import concourse.bass as bass
from concourse import mybir
from contextlib import ExitStack

P = 128
N, F, E, HID = 12500, 64, 212500, 128
T = -(-N // P)
CH = 4
GE = CH * P
G = -(-E // GE)
SLOTS = 8
UN = 2 * SLOTS
GI = G // UN
BLK = 2176
EPAD = T * BLK
KB = BLK // P
XR = 4
TAB = 8
F1 = F + 1
AR = 99 * P
FB = 7
BIG = 3.0e38
assert G % UN == 0 and T % 2 == 0 and EPAD >= G * GE and T % FB == 0


def gnn_kernel(nc, x, dst_line, dst_cols, src_cols, src_rows, ea_t, w0, w1, b1, w2, b2, wfcr, wfc, loop_w, w3b, out):
    fp32, bf16, i32, u32 = mybir.dt.float32, mybir.dt.bfloat16, mybir.dt.int32, mybir.dt.uint32
    ALU = mybir.AluOpType
    ACT = mybir.ActivationFunctionType
    AX = mybir.AxisListType
    ds = bass.ds
    ctx = ExitStack()
    with ctx:
        def sb(name, shape, dt=fp32):
            return ctx.enter_context(nc.sbuf_tensor(name, shape, dt))

        def sem(name):
            return ctx.enter_context(nc.semaphore(name))

        def dram(name, shape, dt=fp32):
            return nc.dram_tensor(name, shape, dt, kind="Internal").ap()

        tables = [dram(f"table{i}", (T * P, F)) for i in range(4)]
        eh_d = dram("eh_d", (T + 1, F, BLK))
        pm_d = dram("pm_d", (T + 1, F, BLK))
        gate_d = dram("gate_d", (EPAD + 64,), bf16)
        ex_d = dram("ex_d", (EPAD, 2 * F))
        accs = [dram(f"acc{i}", (AR, F1)) for i in range(TAB)]

        xs = sb("xs", [P, T, F])
        cat = sb("cat", [P, T, 2 * F])
        dcol = sb("dcol", [P, G * CH])
        scol = sb("scol", [P, G * CH])
        idx = sb("idx", [P, G * CH], i32)
        prior = sb("prior", [P, G * CH])
        dinv = sb("dinv", [P, T])
        has = sb("has", [P, T])
        last = sb("last", [1, T + 1], i32)
        iota = sb("iota", [P, P])
        negt = sb("negt", [P, T])
        tri = sb("tri", [P, P])
        ident = sb("ident", [P, P])
        ones = sb("ones", [P, P])
        zb = sb("zb", [P, 512], bf16)
        epsc = sb("epsc", [P, 1])
        w0s = sb("w0s", [P, F])
        b2s = sb("b2s", [P, F])
        b1s = sb("b1s", [HID, 1])
        w1s = sb("w1s", [2 * F, HID])
        w2s = sb("w2s", [HID, 2 * F])
        wfcrs = sb("wfcrs", [F, F])
        wfcs = sb("wfcs", [F, F])
        lws = sb("lws", [F, F])
        w3s = sb("w3s", [F1, F])
        ring = sb("ring", [P, SLOTS, CH, F])
        stage = sb("stage", [P, 2, SLOTS * CH], i32)
        oh = sb("oh", [P, CH, P])
        exr = sb("exr", [P, XR, CH, 2 * F])
        prod = sb("prod", [P, 2, CH, F])
        big = sb("big", [P, 8 * BLK])

        def bigv(i, n=BLK):
            return big[0:F, i * BLK:i * BLK + n]

        ea = [bigv(0), bigv(1)]
        eh = [bigv(2), bigv(3)]
        pm = [bigv(4), bigv(5)]
        gate = [bigv(6).bitcast(bf16)[:, 0:BLK], bigv(6).bitcast(bf16)[:, BLK:2 * BLK]]
        mx = bigv(7)
        exo = [big[:, 0:BLK], big[:, BLK:2 * BLK]]
        h3 = big[:, 0:T * F1].rearrange("p (t c) -> p t c", c=F1)
        at = T * F1
        srcb = big[:, at:at + XR * GE].bitcast(i32).rearrange("p (s e) -> p s e", s=XR)
        at += XR * GE
        pay = big[:, at:at + SLOTS * CH * F1].rearrange("p (s c) -> p s c", s=SLOTS)
        at += SLOTS * CH * F1
        same = big[:, at:at + 2 * GE].rearrange("p (s e) -> p s e", s=2)
        at += 2 * GE
        pick = big[:, at:at + GE]
        at += GE
        junk = big[:, at:at + GE]
        at += GE
        assert at <= 8 * BLK
        fin0 = T * F1
        fin = [big[:, fin0 + h * TAB * FB * F1:fin0 + (h + 1) * TAB * FB * F1] for h in range(2)]
        exr3 = exr[:, :, :, :].rearrange("p s k c -> p (s k c)")[:, 0:XR * CH * F].rearrange(
            "p (s k c) -> p s k c", s=XR, k=CH)
        carry = sb("carry", [F, 1])
        dst_i = exr[:, :, :, :].rearrange("p s k c -> p (s k c)")[:, 0:G * CH].bitcast(i32)
        dst_b = big[0:T, 0:BLK + 1].bitcast(i32)
        gate_b = big[0:T, 6 * BLK:7 * BLK].bitcast(bf16)[:, 0:BLK]
        GP = G // 4
        g0i, g0f, thr = sb("g0i", [GP, 4], i32), sb("g0f", [GP, 4]), sb("thr", [P, T])
        below = big[0:GP, 7 * BLK:7 * BLK + 4 * T].rearrange("p (a t) -> p a t", a=4)
        nhas = sb("nhas", [P, T])
        spare = sb("spare", [P, 1])
        fac = sb("fac", [P, FB])
        aT = [sb(f"aT{h}", [F1, P]) for h in range(2)]
        dsum = sb("dsum", [P, FB * F1])

        st6 = sb("st6", [P, 6])
        mv = sb("mv", [P, 2])
        sd = sb("sd", [P, 1])
        rs = sb("rs", [P, 1])
        yc = sb("yc", [P, F])
        catw = sb("catw", [P, 2 * F])
        hT = sb("hT", [P, P])
        hidT = sb("hidT", [P, P])
        zT = sb("zT", [F, P])
        hrow = sb("hrow", [P, F])
        trow = sb("trow", [P, F])
        tmp = [sb(f"tmp{i}", [P, F]) for i in range(3)]

        pair = ctx.enter_context(nc.psum_tensor("pair", [P, 2 * 512], fp32))
        bank = [pair[:, 0:512], pair[:, 512:1024]]
        bank += [ctx.enter_context(nc.psum_tensor(f"bank{i}", [P, 512], fp32))[:, :] for i in range(2, 8)]
        pick_ps = bank[2]

        s_const = sem("s_const")
        s_settled = sem("s_settled")
        s_in = sem("s_in")
        s_prep = sem("s_prep")
        s_sq = sem("s_sq")
        s_cnt = sem("s_cnt")
        s_last = sem("s_last")
        s_tab = [sem(f"s_tab{i}") for i in range(4)]
        s_din = sem("s_din")
        s_gate = sem("s_gate")
        s_zero = sem("s_zero")
        landed = [sem(f"landed{i}") for i in range(SLOTS)]
        staged = [sem(f"staged{i}") for i in range(2)]
        exl = [sem(f"exl{i}") for i in range(XR)]
        srl = [sem(f"srl{i}") for i in range(XR)]

        def sems(p, names):
            return {n: sem(f"{n}_{p}") for n in names.split()}

        common = "rows_ready slots_free oh_ready oh_free sums_ready sums_used "
        norm = "stats mvar cent root rroot h_done "
        q = [sems(0, common + norm), sems(1, common + "xb catT hT_rdy hid hid_rdy lin lin_used trow_rdy"),
             sems(2, common + norm + "xd prod_rdy hTp hT_rdy zz zT_rdy u_rdy pre trow_rdy"),
             sems(3, common + norm + "xd pre dup pidx"),
             sems(4, "oh_ready oh_free same_rdy src_rdy pick_rdy rows_done pay_rdy pay_free stage_free")]
        f_ld = [sem(f"f_ld{h}") for h in range(2)]
        f_mm, f_cp, f_scan = sem("f_mm"), sem("f_cp"), sem("f_scan")
        f_st = [sem(f"f_st{h}") for h in range(2)]
        b_ld = [sem(f"b_ld{h}") for h in range(2)]
        b_scan, b_carry, b_d, b_ex, b_tp, b_cp = [sem(n) for n in "b_scan b_carry b_d b_ex b_tp b_cp".split()]
        b_st = [sem(f"b_st{h}") for h in range(2)]
        s_acc = [sem(f"s_acc{h}") for h in range(2)]
        s_ld8 = [sem(f"s_ld8{h}") for h in range(2)]
        z_sum, z_tp, z_cp, z_mm, z_out, z_fac = sem("z_sum"), sem("z_tp"), sem("z_cp"), sem("z_mm"), sem("z_out"), sem("z_fac")
        s_out = sem("s_out")

        NIN = 13
        widths = [(j * 512, min(512, BLK - j * 512)) for j in range(-(-BLK // 512))]
        NJ = len(widths)
        kbat = [list(range(k, min(k + 4, KB))) for k in range(0, KB, 4)]
        NK = len(kbat)

        def settle(eng):
            eng.sem_inc(s_settled, 1)

        def tile_range(eng, t):
            settle(eng)
            a = eng.value_load(last[0:1, ds(t, 1)], min_val=0, max_val=G - 1)
            b = eng.value_load(last[0:1, ds(t + 1, 1)], min_val=0, max_val=G - 1)
            return a, b

        def visits(eng, t, visit):
            a, b = tile_range(eng, t)
            visit(a, a + t, False)
            with eng.If(a < b):
                with eng.Fori(a, b) as g:
                    visit(g + 1, g + t + 1, True)

        marks = {}
        ctx.enter_context(nc.allow_non_contiguous_dma(reason="a few hundred single elements"))
        block = ctx.enter_context(nc.Block())

        @block.gpsimd
        def _(pool):
            pool.memset(ident[:, :], 0.0).then_inc(s_const, 1)
            pool.memset(tri[:, :], 1.0).then_inc(s_const, 1)
            pool.memset(ones[:, :], 1.0).then_inc(s_const, 1)
            pool.memset(prior[:, :], 0.0).then_inc(s_const, 1)
            pool.memset(epsc[:, :], 1e-5).then_inc(s_const, 1)
            pool.memset(zb[:, :], 0.0).then_inc(s_const, 1)
            pool.iota(iota[:, :], pattern=[[1, P]], base=0, channel_multiplier=0,
                      allow_small_or_imprecise_dtypes=True).then_inc(s_const, 1)
            pool.iota(negt[:, :], pattern=[[-P, T]], base=0, channel_multiplier=0,
                      allow_small_or_imprecise_dtypes=True).then_inc(s_const, 1)
            pool.iota(thr[:, :], pattern=[[P, T]], base=P, channel_multiplier=0,
                      allow_small_or_imprecise_dtypes=True).then_inc(s_const, 1)
            pool.iota(spare[:, :], pattern=[[0, 1]], base=N, channel_multiplier=1,
                      allow_small_or_imprecise_dtypes=True).then_inc(s_const, 1)
            pool.wait_ge(s_const, 10)
            pool.affine_select(out=ident[:, :], in_=ident[:, :], compare_op=ALU.not_equal, fill=1.0, base=0,
                               pattern=[[-1, P]], channel_multiplier=1).then_inc(s_const, 1)
            pool.affine_select(out=tri[:, :], in_=tri[:, :], compare_op=ALU.is_gt, fill=0.0, base=0,
                               pattern=[[-1, P]], channel_multiplier=1).then_inc(s_const, 1)

            for p in range(4):
                s = q[p]
                pool.sem_inc(s["slots_free"], SLOTS)
                pool.wait_ge(s_tab[p], 16 * (1 if p == 0 else T))
                with pool.Fori(0, GI) as i:
                    for u in range(UN):
                        st, slot = divmod(u, SLOTS)
                        if slot == 0:
                            pool.wait_ge(staged[st], i * 16 + 16 * (GI * p + 1))
                        pool.wait_ge(s["slots_free"], i * UN + u + 1)
                        settle(pool)
                        for k in range(CH):
                            c = slot * CH + k
                            pool.indirect_dma_start(
                                out=ring[:, slot, k, :], out_offset=None, in_=tables[p],
                                in_offset=bass.IndirectOffsetOnAxis(ap=stage[:, st, c:c + 1].bitcast(u32), axis=0),
                            ).then_inc(landed[slot], 16)

            s = q[4]
            pool.wait_ge(s_zero, 16 * TAB)
            with pool.Fori(0, GI) as i:
                for u in range(UN):
                    st, slot = divmod(u, SLOTS)
                    if slot == 0:
                        pool.wait_ge(staged[st], i * 16 + 16 * (GI * 4 + 1))
                    pool.wait_ge(s_acc[u % 2], i * (CH * 16 * SLOTS) + CH * 16 * (u // 2))
                    pool.sem_inc(s["pay_free"], 1)
                    if slot == 1:
                        pool.sem_inc(s["stage_free"], 1)
                    pool.wait_ge(s["pay_rdy"], i * UN + u + 1)
                    settle(pool)
                    for k in range(CH):
                        c = slot * CH + k
                        pool.indirect_dma_start(
                            out=accs[CH * (u % 2) + k],
                            out_offset=bass.IndirectOffsetOnAxis(ap=stage[:, st, c:c + 1].bitcast(u32), axis=0),
                            in_=pay[:, slot, k * F1:(k + 1) * F1], in_offset=None, compute_op=ALU.add,
                        ).then_inc(s_acc[u % 2], 16)

        @block.sync
        def _(sp):
            sp.dma_start(xs[:, :, :], x).then_inc(s_in, 16)
            sp.dma_start(idx[:, :], src_cols).then_inc(s_in, 16)
            sp.dma_start(g0i[:, :], dst_line[1:1 + G * GE].rearrange("(p q e) -> p q e", q=4, e=GE)[:, :, 0]).then_inc(s_in, 16)
            sp.dma_start(w0s[:, :], w0.partition_broadcast(P)).then_inc(s_in, 16)
            sp.dma_start(b2s[:, :], b2.partition_broadcast(P)).then_inc(s_in, 16)
            sp.dma_start(b1s[:, :], b1).then_inc(s_in, 16)
            for dst, src in ((w1s, w1), (w2s, w2), (wfcrs, wfcr), (wfcs, wfc), (lws, loop_w), (w3s, w3b)):
                sp.dma_start(dst[:, :], src).then_inc(s_in, 16)
            sp.dma_start(dst_i, dst_cols).then_inc(s_in, 16)

            sp.wait_ge(s_const, 4)
            for a in accs:
                sp.dma_start(a.rearrange("(p b c) f -> p b (c f)", b=9, c=11),
                             prior[:, 0:11 * F1].unsqueeze(1).to_broadcast([P, 9, 11 * F1])).then_inc(s_zero, 16)

            def load_stage(st, g0):
                settle(sp)
                sp.dma_start(stage[:, st, :], idx[:, ds(g0 * CH, SLOTS * CH)]).then_inc(staged[st], 16)

            def load_ex(p, slot, g):
                settle(sp)
                rows = ex_d[ds(g * GE, GE), :].rearrange("(p k) c -> p k c", k=CH)
                if p == 2:
                    sp.dma_start(exr[:, slot, :, :], rows).then_inc(exl[slot], 16)
                else:
                    sp.dma_start(exr3[:, slot, :, :], rows[:, :, 0:F]).then_inc(exl[slot], 16)

            def load_src(slot, g):
                settle(sp)
                sp.dma_start(srcb[:, slot, :], src_rows[ds(g * GE, GE)].partition_broadcast(P)).then_inc(srl[slot], 16)

            sp.wait_ge(s_in, 16 * NIN)
            load_stage(0, 0)
            load_stage(1, SLOTS)
            for p in range(4):
                s = q[p]
                if p == 2:
                    for h in range(2):
                        sp.wait_ge(b_st[h], 16 * (T // 2))
                if p == 3:
                    sp.wait_ge(q[2]["pre"], 4 * T)
                if p >= 2:
                    load_ex(p, 0, 0)
                    load_ex(p, 1, 1)
                if p == 3:
                    sp.sem_inc(s["dup"], 2 * CH)
                    load_src(0, 0)
                    load_src(1, 1)

                def step(i, u, final):
                    g = i * UN + u
                    slot = u % SLOTS
                    sp.wait_ge(landed[slot], i * (2 * CH * 16) + CH * 16 * (2 * GI * p + u // SLOTS + 1))
                    if p >= 2:
                        settle(sp)
                        sp.wait_ge(exl[u % XR], i * (16 * UN // XR) + 16 * ((p - 2) * (G // XR) + u // XR + 1))
                    if p == 3:
                        settle(sp)
                        sp.wait_ge(srl[u % XR], i * (16 * UN // XR) + 16 * (u // XR + 1))
                    sp.sem_inc(s["rows_ready"], 1)
                    if slot == SLOTS - 1 and not (p == 3 and final):
                        load_stage(u // SLOTS, (u - slot) if final else (i + 1) * UN + (u - slot))
                    if p >= 2 and not (final and u >= UN - 2):
                        sp.wait_ge(s["slots_free"], i * UN + u - 1 + SLOTS)
                        load_ex(p, (u + 2) % XR, g + 2)
                    if p == 3 and not (final and u >= UN - 2):
                        sp.wait_ge(s["dup"], i * UN * CH + CH * u + CH)
                        load_src((u + 2) % XR, g + 2)

                with sp.Fori(0, GI - 1) as i:
                    for u in range(UN):
                        step(i, u, False)
                for u in range(UN):
                    step(GI - 1, u, True)

            s = q[4]
            sp.wait_ge(q[3]["pidx"], 6)
            load_stage(0, 0)
            sp.sem_inc(s["same_rdy"], 2 * CH)
            load_src(0, 0)
            load_src(1, 1)

            def step4(i, u, final):
                sp.wait_ge(srl[u % XR], i * (16 * UN // XR) + 16 * (G // XR + u // XR + 1))
                sp.sem_inc(s["src_rdy"], 1)
                if u == 4:
                    sp.wait_ge(s["stage_free"], i * 2 + 1)
                    load_stage(1, i * UN + SLOTS)
                if u == 12 and not final:
                    sp.wait_ge(s["stage_free"], i * 2 + 2)
                    load_stage(0, i * UN + UN)
                if not (final and u >= UN - 2):
                    sp.wait_ge(s["same_rdy"], i * UN * CH + CH * u + CH)
                    load_src((u + 2) % XR, i * UN + u + 2)

            with sp.Fori(0, GI - 1) as i:
                for u in range(UN):
                    step4(i, u, False)
            for u in range(UN):
                step4(GI - 1, u, True)
            for h in range(2):
                sp.wait_ge(s_acc[h], CH * 16 * G // 2)
            with sp.Fori(0, T // FB // 2) as i:
                for h in range(2):
                    sp.wait_ge(z_sum, i * 2 + (h + 1))
                    settle(sp)
                    for k in range(TAB):
                        sp.dma_start(fin[h][:, k * FB * F1:(k + 1) * FB * F1].rearrange("p (t c) -> p t c", c=F1),
                                     accs[k][ds((i * 2 + h) * (FB * P), FB * P), :].rearrange("(t p) c -> p t c", p=P)
                                     ).then_inc(s_ld8[h], 16)
            sp.wait_ge(s_out, 16 * (T // FB))

        @block.vector
        def _(dve):
            steps = [0]

            def link(ins):
                steps[0] += 1
                ins.then_inc(s_prep, 1)
                dve.wait_ge(s_prep, steps[0])
                return steps[0]

            V = nc.vector
            dve.wait_ge(s_const, 12)
            dve.wait_ge(s_in, 16 * NIN)
            xc, h0 = cat[:, :, 0:F], cat[:, :, F:2 * F]

            def over(col):
                return col[:, :].unsqueeze(2).to_broadcast([P, T, F])
            link(V.tensor_reduce(has[:, :], xs[:, :, :], AX.X, ALU.add))
            link(V.tensor_scalar(has[:, :], has[:, :], 1.0 / F, None, ALU.mult))
            link(V.tensor_tensor(xc, xs[:, :, :], over(has), ALU.subtract))
            link(V.tensor_tensor(h0, xc, xc, ALU.mult))
            marks["var"] = link(V.tensor_reduce(dinv[:, :], h0, AX.X, ALU.add))
            link(V.tensor_copy(scol[:, :], idx[:, :]))
            link(V.tensor_copy(dcol[:, :], dst_i))
            link(V.tensor_copy(g0f[:, :], g0i[:, :]))
            for a in range(4):
                marks["below"] = link(V.tensor_scalar(below[:, a, :], thr[0:GP, :], g0f[:, a:a + 1], None, ALU.is_gt))
            dve.wait_ge(s_sq, 1)
            link(V.reciprocal(dinv[:, :], nhas[:, :]))
            link(V.tensor_tensor(xc, xc, over(dinv), ALU.mult))
            marks["tab"] = link(V.scalar_tensor_tensor(h0, xc, 0.0, w0s[:, :].unsqueeze(1).to_broadcast([P, T, F]), ALU.max, ALU.mult))
            dve.wait_ge(s_cnt, 1)
            link(V.memset(last[0:1, 0:1], 0))
            link(V.tensor_scalar(last[0:1, 1:T + 1], bank[6][0:1, 0:T], 1.0, -1.0, ALU.max, ALU.add))
            dve.sem_inc(s_last, 1)
            dve.wait_ge(s_din, 32)
            link(V.tensor_tensor(gate_b, dst_b[:, 1:BLK + 1], dst_b[:, 0:BLK], ALU.is_equal))
            marks["gate"] = link(V.tensor_scalar(gate_b, gate_b, -1.0, BIG, ALU.add, ALU.mult))
            link(V.memset(eh[1], 0.0))
            marks["end"] = link(V.memset(pm[1], 0.0))

            def build(p, g, v, t):
                s = q[p]
                for k in range(CH):
                    dve.wait_ge(s["oh_free"], v * CH + (k + 1))
                    V.tensor_scalar(oh[:, k, :], iota[:, :], dcol[:, ds(g * CH + k, 1)], negt[:, ds(t, 1)],
                                    ALU.subtract, ALU.is_equal).then_inc(s["oh_ready"], 1)

            def stats(p, t, h=None):
                s = q[p]
                settle(dve)
                V.bn_stats(st6[:, :], xs[:, ds(t, 1), :].rearrange("p a c -> p (a c)")).then_inc(s["stats"], 1)
                dve.wait_ge(s["stats"], t + 1)
                settle(dve)
                V.bn_aggr(mv[:, :], st6[:, :]).then_inc(s["mvar"], 1)
                dve.wait_ge(s["mvar"], t + 1)
                V.tensor_scalar(yc[:, :], xs[:, ds(t, 1), :].rearrange("p a c -> p (a c)"), mv[:, 0:1], 0.0,
                                ALU.subtract, ALU.max).then_inc(s["cent"], 1)

            def rroot(p, t):
                s = q[p]
                dve.wait_ge(s["root"], t + 1)
                V.reciprocal(rs[:, :], sd[:, :]).then_inc(s["rroot"], 1)

            def row(tile, t, a=0, b=F):
                return tile[:, ds(t, 1), a:b].rearrange("p o c -> p (o c)")

            s = q[0]
            with dve.Fori(0, T // 2) as i:
                for h in range(2):
                    t = i * 2 + h

                    def visit(g, v, new):
                        build(0, g, v, t)
                        if new:
                            dve.sem_inc(s["slots_free"], 1)
                    visits(dve, t, visit)
                    dve.wait_ge(s["sums_ready"], t + 1)
                    V.tensor_copy(has[:, ds(t, 1)], bank[h][:, F:F + 1])
                    V.tensor_tensor(row(xs, t), row(xs, t), bank[h][:, 0:F], ALU.add).then_inc(s["sums_used"], 1)
                    dve.wait_ge(s["sums_used"], t + 3)
                    dve.wait_ge(s["h_done"], t)
                    stats(0, t)
                    dve.wait_ge(f_cp, t * NJ + NJ)
                    dve.wait_ge(f_ld[h], i * 32 + 32)
                    dve.wait_ge(f_st[h], i * 32 + 32 * h)
                    dve.wait_ge(f_scan, t)
                    V.tensor_tensor_scan(pm[h], gate[h], eh[h], pm[1 - h][:, BLK - 1:BLK], ALU.add, ALU.max).then_inc(f_scan, 1)
                    rroot(0, t)
            link(V.tensor_scalar(dinv[:, :], has[:, :], 1.0, None, ALU.max))
            link(V.reciprocal(dinv[:, :], dinv[:, :]))
            link(V.tensor_scalar(has[:, :], has[:, :], 1.0, None, ALU.min))
            link(V.tensor_scalar(nhas[:, :], has[:, :], -1.0, 1.0, ALU.mult, ALU.add))
            link(V.memset(carry[:, :], 0.0))

            s1 = q[1]
            with dve.Fori(0, T // 2) as i:
                for h in range(2):
                    t = i * 2 + h

                    def visit(g, v, new):
                        build(1, g, v, t)
                        if new:
                            dve.sem_inc(s1["slots_free"], 1)
                    visits(dve, t, visit)
                    dve.wait_ge(b_ld[h], i * 48 + 48)
                    dve.wait_ge(b_carry, t)
                    dve.wait_ge(b_d, t)
                    V.tensor_tensor_scan(mx[:, BLK - 1::-1], gate[h][:, BLK - 1::-1], pm[h][:, BLK - 1::-1],
                                         carry[:, :], ALU.add, ALU.max).then_inc(b_scan, 1)
                    dve.wait_ge(b_scan, t + 1)
                    V.tensor_copy(carry[:, :], mx[:, 0:1]).then_inc(b_carry, 1)
                    V.tensor_tensor(pm[h], eh[h], mx, ALU.subtract).then_inc(b_d, 1)
                    V.tensor_tensor(row(xs, t), row(xs, t), b2s[:, :], ALU.add).then_inc(s1["xb"], 1)
                    dve.wait_ge(s1["catT"], t)
                    V.tensor_copy(catw[:, F:2 * F], row(cat, t, F, 2 * F)).then_inc(s1["xb"], 1)
                    dve.wait_ge(s1["sums_ready"], t + 1)
                    V.tensor_scalar(catw[:, 0:F], bank[h][:, 0:F], dinv[:, ds(t, 1)], None, ALU.mult).then_inc(s1["sums_used"], 1)
                    dve.wait_ge(s1["xb"], t * 2 + 2)
                    dve.wait_ge(s1["lin"], t + 1)
                    V.tensor_tensor(row(xs, t), row(xs, t), bank[6][:, P + F:2 * P], ALU.add).then_inc(s1["lin_used"], 1)

            s2 = q[2]

            def edge_product(g):
                dve.wait_ge(s2["rows_ready"], g + 1)
                slot = g % XR
                e, c = [exr[:, ds(slot, 1), :, a * F:a * F + F].rearrange("p o k c -> p (o k) c") for a in range(2)]
                V.tensor_tensor(c, c, e, ALU.mult).then_inc(s2["prod_rdy"], 1)
            edge_product(0)
            with dve.Fori(0, T // 2) as i:
                for h in range(2):
                    t = i * 2 + h

                    def visit(g, v, new):
                        if new:
                            edge_product(g)
                        build(2, g, v, t)
                        if new:
                            dve.sem_inc(s2["slots_free"], 1)
                    visits(dve, t, visit)
                    dve.wait_ge(s2["sums_ready"], t + 1)
                    V.scalar_tensor_tensor(row(xs, t), bank[h][:, 0:F], dinv[:, ds(t, 1)], row(xs, t),
                                           ALU.mult, ALU.add).then_inc(s2["xd"], 1)
                    dve.wait_ge(s2["xd"], t + 1)
                    dve.wait_ge(s2["h_done"], t)
                    stats(2, t)
                    NP = 4

                    def pre(n, ins):
                        ins.then_inc(s2["pre"], 1)
                        dve.wait_ge(s2["pre"], t * NP + n)
                    pre(1, V.tensor_scalar(tmp[0][:, :], bank[h][:, F:2 * F], 0.5, None, ALU.max))
                    pre(2, V.reciprocal(tmp[1][:, :], tmp[0][:, :]))
                    rroot(2, t)
                    V.tensor_scalar(row(cat, t), tmp[1][:, :], has[:, ds(t, 1)], None, ALU.mult)
                    V.tensor_tensor(tmp[0][:, :], bank[h][:, 2 * F:3 * F], tmp[1][:, :], ALU.mult).then_inc(s2["sums_used"], 1)
                    dve.wait_ge(s2["sums_used"], t + 3)
                    dve.wait_ge(s2["u_rdy"], t + 1)
                    dve.wait_ge(s2["trow_rdy"], t + 1)
                    V.tensor_scalar(tmp[2][:, :], bank[6][:, P:P + F], nhas[:, ds(t, 1)], None, ALU.mult)
                    pre(3, V.tensor_tensor(tmp[0][:, :], tmp[0][:, :], bank[7][:, P:P + F], ALU.add))
                    pre(4, V.scalar_tensor_tensor(row(cat, t, F, 2 * F), tmp[0][:, :], has[:, ds(t, 1)], tmp[2][:, :],
                                                  ALU.mult, ALU.add))

            s3 = q[3]
            V.memset(h3[:, :, F:F1], 1.0).then_inc(s3["pidx"], 1)

            def weigh(g):
                dve.wait_ge(s3["rows_ready"], g + 1)
                V.tensor_tensor(prod[:, ds(g % 2, 1), :, :].rearrange("p o k c -> p (o k c)"),
                                ring[:, ds(g % SLOTS, 1), :, :].rearrange("p o k c -> p (o k c)"),
                                exr3[:, ds(g % XR, 1), :, :].rearrange("p o k c -> p (o k c)"),
                                ALU.mult).then_inc(s3["slots_free"], 1)
                for k in range(CH):
                    dve.wait_ge(s3["dup"], g * CH + (k + 1 + CH))
                    V.scalar_tensor_tensor(junk[:, k * P:(k + 1) * P], srcb[:, ds(g % XR, 1), k * P:(k + 1) * P].rearrange("p o e -> p (o e)"),
                                           scol[:, ds(g * CH + k, 1)], tri[:, :], ALU.is_equal, ALU.mult,
                                           accum_out=prior[:, ds(g * CH + k, 1)]).then_inc(s3["dup"], 1)
            weigh(0)
            with dve.Fori(0, T // 2) as i:
                for h in range(2):
                    t = i * 2 + h

                    def visit(g, v, new):
                        if new:
                            weigh(g)
                        build(3, g, v, t)
                    visits(dve, t, visit)
                    dve.wait_ge(s3["sums_ready"], t + 1)
                    V.tensor_tensor(tmp[0][:, :], bank[h][:, 0:F], row(cat, t), ALU.mult).then_inc(s3["sums_used"], 1)
                    dve.wait_ge(s3["sums_used"], t + 3)
                    V.tensor_tensor(tmp[1][:, :], tmp[0][:, :], row(cat, t, F, 2 * F), ALU.add).then_inc(s3["pre"], 1)
                    dve.wait_ge(s3["pre"], t + 1)
                    V.scalar_tensor_tensor(row(xs, t), tmp[1][:, :], 0.0, row(xs, t), ALU.max, ALU.add).then_inc(s3["xd"], 1)
                    dve.wait_ge(s3["xd"], t + 1)
                    dve.wait_ge(s3["h_done"], t)
                    stats(3, t)
                    rroot(3, t)

            def pstep(n, ins):
                ins.then_inc(s3["pidx"], 1)
                dve.wait_ge(s3["pidx"], n)
            to = exr[:, :, :, :].rearrange("p s k c -> p (s k c)")[:, 0:G * CH]
            dve.wait_ge(s3["dup"], G * CH + 2 * CH)
            pstep(2, V.tensor_scalar(prior[:, :], prior[:, :], 0.5, None, ALU.is_gt))
            pstep(3, V.tensor_scalar(to, scol[:, :], -1.0, spare[:, :], ALU.mult, ALU.add))
            pstep(4, V.tensor_tensor(to, to, prior[:, :], ALU.mult))
            pstep(5, V.tensor_tensor(to, to, scol[:, :], ALU.add))
            pstep(6, V.tensor_copy(idx[:, :], to))

            s4 = q[4]

            def equal_src(g):
                dve.wait_ge(s4["src_rdy"], g + 1)
                for k in range(CH):
                    V.tensor_scalar(same[:, ds(g % 2, 1), k * P:(k + 1) * P].rearrange("p o e -> p (o e)"),
                                    srcb[:, ds(g % XR, 1), k * P:(k + 1) * P].rearrange("p o e -> p (o e)"),
                                    scol[:, ds(g * CH + k, 1)], None, ALU.is_equal).then_inc(s4["same_rdy"], 1)
            equal_src(0)
            with dve.Fori(0, T) as t:
                def visit(g, v, new):
                    if new:
                        equal_src(g)
                    build(4, g, v, t)
                visits(dve, t, visit)

            dve.sem_inc(z_sum, 2)
            with dve.Fori(0, T // FB // 2) as i:
                for h in range(2):
                    m = i * 2 + h
                    dve.wait_ge(s_ld8[h], i * (16 * TAB) + 16 * TAB)
                    dve.wait_ge(z_tp, m * FB)
                    V.tensor_reduce(dsum[:, :], fin[h].rearrange("p (a c) -> p c a", a=TAB), AX.X, ALU.add).then_inc(z_sum, 1)
                    dve.wait_ge(z_sum, m + 3)
                    V.tensor_scalar(fac[:, :], dsum[:, F::F1], 1.0, None, ALU.max).then_inc(z_fac, 1)
                    dve.wait_ge(z_fac, m * 2 + 1)
                    V.reciprocal(fac[:, :], fac[:, :]).then_inc(z_fac, 1)
                    dve.wait_ge(z_fac, m * 2 + 2)
                    for a in range(FB):
                        dve.wait_ge(z_mm, m * FB + (a + 1))
                        r = row(xs, m * FB + a)
                        V.scalar_tensor_tensor(r, bank[5 + (h * FB + a) % 2][:, 0:F], fac[:, a:a + 1], r,
                                               ALU.mult, ALU.add).then_inc(z_out, 1)

        @block.scalar
        def _(act):
            S = nc.scalar

            def row(tile, t, a=0, b=F):
                return tile[:, ds(t, 1), a:b].rearrange("p o c -> p (o c)")

            act.dma_start(dst_b[:, 1:BLK + 1], dst_line[1:1 + EPAD].rearrange("(b e) -> b e", e=BLK)).then_inc(s_din, 16)
            act.dma_start(dst_b[:, 0:1], dst_line[0:EPAD].rearrange("(b e) -> b e", e=BLK)[:, 0:1]).then_inc(s_din, 16)
            act.wait_ge(s_const, 12)
            act.dma_start(gate_d[EPAD:EPAD + 64].rearrange("(o e) -> o e", o=1), zb[0:1, 0:64]).then_inc(s_gate, 16)
            act.wait_ge(s_prep, marks["var"])
            S.activation(nhas[:, :], dinv[:, :], ACT.Sqrt, bias=epsc[:, :], scale=1.0 / F).then_inc(s_sq, 1)
            act.wait_ge(s_prep, marks["tab"])
            act.dma_start(tables[0].rearrange("(t p) c -> p t c", p=P), cat[:, :, F:2 * F]).then_inc(s_tab[0], 16)
            act.wait_ge(s_prep, marks["gate"])
            act.dma_start(gate_d[0:EPAD].rearrange("(b e) -> b e", e=BLK), gate_b).then_inc(s_gate, 16)
            act.wait_ge(s_gate, 32)
            act.wait_ge(s_prep, marks["end"])

            def load_f(h, b):
                act.dma_start(ea[h], ea_t[:, ds(b * BLK, BLK)]).then_inc(f_ld[h], 16)
                act.dma_start(gate[h], gate_d[ds(b * BLK, BLK)].partition_broadcast(F)).then_inc(f_ld[h], 16)

            def store_f(h, b1):
                act.dma_start(eh_d[ds(b1, 1), :, :].rearrange("o c e -> (o c) e"), eh[h]).then_inc(f_st[h], 16)
                act.dma_start(pm_d[ds(b1, 1), :, :].rearrange("o c e -> (o c) e"), pm[h]).then_inc(f_st[h], 16)

            def norm_end(p, t, dst):
                s = q[p]
                act.wait_ge(s["mvar"], t + 1)
                S.activation(sd[:, :], mv[:, 1:2], ACT.Sqrt, bias=epsc[:, :], scale=1.0).then_inc(s["root"], 1)
                act.wait_ge(s["rroot"], t + 1)
                act.wait_ge(s["cent"], t + 1)
                S.activation(dst, yc[:, :], ACT.Copy, scale=rs[:, :]).then_inc(s["h_done"], 1)

            load_f(0, 0)
            s = q[0]

            def tile0(i, h, final):
                t = i * 2 + h
                act.wait_ge(f_scan, t)
                store_f(1 - h, t)
                if not final:
                    load_f(1 - h, t + 1)
                act.wait_ge(f_st[h], i * 32 + 32 * h)
                for j, (e0, n) in enumerate(widths):
                    act.wait_ge(f_mm, t * NJ + (j + 1))
                    S.activation(eh[h][:, e0:e0 + n], bank[2 + j % 4][0:F, 0:n], ACT.Copy).then_inc(f_cp, 1)
                norm_end(0, t, row(cat, t, F, 2 * F))
                act.wait_ge(s["h_done"], t + 1)
                act.dma_start(tables[1][ds(t * P, P), :], row(cat, t, F, 2 * F)).then_inc(s_tab[1], 16)
            with act.Fori(0, T // 2 - 1) as i:
                for h in range(2):
                    tile0(i, h, False)
            for h in range(2):
                tile0(T // 2 - 1, h, h == 1)
            act.wait_ge(f_scan, T)
            store_f(1, T)

            s1 = q[1]
            act.wait_ge(f_st[0], 32 * (T // 2))
            act.wait_ge(f_st[1], 32 * (T // 2 + 1))

            def load_b(h, b):
                act.dma_start(eh[h], eh_d[ds(b + 1, 1), :, :].rearrange("o c e -> (o c) e")).then_inc(b_ld[h], 16)
                act.dma_start(pm[h], pm_d[ds(b + 1, 1), :, :].rearrange("o c e -> (o c) e")).then_inc(b_ld[h], 16)
                act.dma_start(gate[h], gate_d[ds(b * BLK + 1, BLK)].partition_broadcast(F)).then_inc(b_ld[h], 16)
            load_b(0, T - 1)

            def tile1(i, h, final):
                t = i * 2 + h
                b = T - 1 - t if isinstance(t, int) else t * -1 + (T - 1)
                if not final:
                    act.wait_ge(b_tp, t * NK)
                    act.wait_ge(b_scan, t)
                    load_b(1 - h, b - 1)
                act.wait_ge(b_d, t + 1)
                S.activation(pm[h], pm[h], ACT.Exp).then_inc(b_ex, 1)
                act.wait_ge(s1["catT"], t + 1)
                S.activation(hT[:, :], bank[6][:, 0:P], ACT.Copy).then_inc(s1["hT_rdy"], 1)
                act.wait_ge(b_st[h], i * 16)
                for j, ks in enumerate(kbat):
                    act.wait_ge(b_tp, t * NK + (j + 1))
                    S.activation(exo[h][:, ks[0] * P:(ks[-1] + 1) * P], bank[2 + j % 4][:, 0:len(ks) * P],
                                 ACT.Copy).then_inc(b_cp, 1)
                act.wait_ge(s1["hid"], t + 1)
                S.activation(hidT[:, :], bank[7][:, 0:P], ACT.Relu, bias=b1s[:, :], scale=1.0).then_inc(s1["hid_rdy"], 1)
                act.wait_ge(b_cp, t * NK + NK)
                act.dma_start(ex_d[ds(b * BLK, BLK), :].rearrange("(p k) c -> p (k c)", k=KB), exo[h]).then_inc(b_st[h], 16)
                act.wait_ge(s1["lin_used"], t + 1)
                act.wait_ge(s_tab[2], t * 16)
                S.activation(trow[:, :], bank[6][:, P:P + F], ACT.Copy).then_inc(s1["trow_rdy"], 1)
                act.wait_ge(s1["trow_rdy"], t + 1)
                act.dma_start(tables[2][ds(t * P, P), :], trow[:, :]).then_inc(s_tab[2], 16)
            with act.Fori(0, T // 2 - 1) as i:
                for h in range(2):
                    tile1(i, h, False)
            for h in range(2):
                tile1(T // 2 - 1, h, h == 1)

            s2 = q[2]
            act.wait_ge(s_tab[2], T * 16)
            with act.Fori(0, T) as t:
                norm_end(2, t, hrow[:, :])
                act.wait_ge(s2["hTp"], t + 1)
                S.activation(hT[0:F, :], bank[6][0:F, 0:P], ACT.Copy).then_inc(s2["hT_rdy"], 1)
                act.wait_ge(s2["zz"], t + 1)
                S.activation(zT[:, :], bank[7][0:F, 0:P], ACT.Copy).then_inc(s2["zT_rdy"], 1)
                act.wait_ge(s_tab[3], t * 16)
                S.activation(trow[:, :], bank[6][:, P:P + F], ACT.Copy).then_inc(s2["trow_rdy"], 1)
                act.wait_ge(s2["trow_rdy"], t + 1)
                act.dma_start(tables[3][ds(t * P, P), :], trow[:, :]).then_inc(s_tab[3], 16)

            with act.Fori(0, T) as t:
                norm_end(3, t, row(h3, t))

            s4 = q[4]
            act.sem_inc(s4["pay_free"], SLOTS - 2)

            def evacuate(g):
                act.wait_ge(s4["rows_done"], g + 1)
                act.wait_ge(s4["pay_free"], g + 1)
                S.activation(pay[:, ds(g % SLOTS, 1), :].rearrange("p o c -> p (o c)"),
                             pair[:, ds((g % 2) * 512, CH * F1)], ACT.Copy).then_inc(s4["pay_rdy"], 1)
            with act.Fori(0, T) as t:
                def visit(g, v, new):
                    if new:
                        evacuate(g - 1)
                    act.wait_ge(s4["oh_free"], v * CH + 2 * CH)
                    S.activation(pick, pick_ps, ACT.Copy).then_inc(s4["pick_rdy"], 1)
                visits(act, t, visit)
            evacuate(G - 1)

            with act.Fori(0, T // FB // 2) as i:
                for h in range(2):
                    m = i * 2 + h
                    for a in range(FB):
                        par = (h * FB + a) % 2
                        act.wait_ge(z_tp, m * FB + (a + 1))
                        S.activation(aT[par][:, :], bank[3 + par][0:F1, 0:P], ACT.Copy).then_inc(z_cp, 1)
                    act.wait_ge(z_out, m * FB + FB)
                    act.dma_start(out[:, ds(m * FB, FB), :], xs[:, ds(m * FB, FB), :]).then_inc(s_out, 16)

        @block.tensor
        def _(pe):
            M = nc.tensor.matmul
            pe.wait_ge(s_const, 12)
            pe.wait_ge(s_prep, marks["below"])
            for a in range(4):
                last_mm = M(bank[6][0:1, 0:T], ones[0:GP, 0:1], below[:, a, :], start=(a == 0), stop=(a == 3))
            last_mm.then_inc(s_cnt, 1)
            pe.wait_ge(s_last, 1)

            def sums(p, t, h, width):
                s = q[p]
                pe.wait_ge(s["sums_used"], t + 1)
                M(bank[h][:, 0:width], zb[:, 0:P], zb[:, 0:width], start=True, stop=False)

                def visit(g, v, new):
                    if p == 2:
                        pe.wait_ge(s["prod_rdy"], g + 1)
                    elif p == 3:
                        pe.wait_ge(s["slots_free"], g + 1 + SLOTS)
                    else:
                        pe.wait_ge(s["rows_ready"], g + 1)
                    for k in range(CH):
                        pe.wait_ge(s["oh_ready"], v * CH + (k + 1))
                        if p == 3:
                            rows = prod[:, ds(g % 2, 1), k, :]
                        else:
                            rows = ring[:, ds(g % SLOTS, 1), k, :]
                        mm = M(bank[h][:, 0:F], oh[:, k, :], rows.rearrange("p o c -> p (o c)"), start=False, stop=False)
                        if p == 0:
                            mm = M(bank[h][:, F:F + 1], oh[:, k, :], ones[:, 0:1], start=False, stop=False)
                        if p == 2:
                            mm = M(bank[h][:, F:3 * F], oh[:, k, :],
                                   exr[:, ds(g % XR, 1), k, :].rearrange("p o c -> p (o c)"), start=False, stop=False)
                        mm.then_inc(s["oh_free"], 1)
                visits(pe, t, visit)
                M(bank[h][:, 0:width], zb[:, 0:P], zb[:, 0:width], start=False, stop=True).then_inc(s["sums_ready"], 1)

            def credit(p):
                pe.sem_inc(q[p]["oh_free"], CH)
                if p < 4:
                    pe.sem_inc(q[p]["sums_used"], 2)

            credit(0)
            with pe.Fori(0, T // 2) as i:
                for h in range(2):
                    t = i * 2 + h
                    sums(0, t, h, F + 1)
                    pe.wait_ge(f_ld[h], i * 32 + 32)
                    for j, (e0, n) in enumerate(widths):
                        if j in (0, 4):
                            pe.wait_ge(f_cp, t * NJ + j // 4)
                            settle(pe)
                        M(bank[2 + j % 4][0:F, 0:n], wfcrs[:, :], ea[h][:, e0:e0 + n], start=True, stop=True).then_inc(f_mm, 1)

            credit(1)
            s1 = q[1]
            with pe.Fori(0, T // 2) as i:
                for h in range(2):
                    t = i * 2 + h
                    sums(1, t, h, F)
                    pe.wait_ge(s1["sums_used"], t + 3)
                    pe.wait_ge(s1["xb"], t * 2 + 2)
                    pe.wait_ge(s1["trow_rdy"], t)
                    nc.tensor.transpose(bank[6][:, 0:P], catw[:, :], ident[:, :]).then_inc(s1["catT"], 1)
                    pe.wait_ge(b_ex, t + 1)
                    settle(pe)
                    for j, ks in enumerate(kbat):
                        if j in (0, 4):
                            pe.wait_ge(b_cp, t * NK + j // 4)
                            settle(pe)
                        for n, k in enumerate(ks):
                            nc.tensor.transpose(bank[2 + j % 4][:, n * P:n * P + F], pm[h][:, k::KB], ident[0:F, 0:F])
                            mm = nc.tensor.transpose(bank[2 + j % 4][:, n * P + F:(n + 1) * P], eh[h][:, k::KB], ident[0:F, 0:F])
                        mm.then_inc(b_tp, 1)
                    pe.wait_ge(s1["hT_rdy"], t + 1)
                    M(bank[7][:, 0:P], w1s[:, :], hT[:, :], start=True, stop=True).then_inc(s1["hid"], 1)
                    pe.wait_ge(s1["hid_rdy"], t + 1)
                    M(bank[6][:, P:2 * P], hidT[:, :], w2s[:, :], start=True, stop=True).then_inc(s1["lin"], 1)

            credit(2)
            s2 = q[2]
            with pe.Fori(0, T // 2) as i:
                for h in range(2):
                    t = i * 2 + h
                    sums(2, t, h, 3 * F)
                    pe.wait_ge(s2["pre"], t * 4)
                    pe.wait_ge(s2["h_done"], t + 1)
                    settle(pe)
                    nc.tensor.transpose(bank[6][0:F, 0:P], hrow[:, :], ident[:, :]).then_inc(s2["hTp"], 1)
                    pe.wait_ge(s2["hT_rdy"], t + 1)
                    M(bank[6][:, P:P + F], hT[0:F, :], wfcs[:, :], start=True, stop=True)
                    M(bank[7][0:F, 0:P], wfcs[:, :], hT[0:F, :], start=True, stop=True).then_inc(s2["zz"], 1)
                    pe.wait_ge(s2["zT_rdy"], t + 1)
                    settle(pe)
                    M(bank[7][:, P:P + F], zT[:, :], lws[:, :], start=True, stop=True).then_inc(s2["u_rdy"], 1)

            credit(3)
            with pe.Fori(0, T // 2) as i:
                for h in range(2):
                    sums(3, i * 2 + h, h, F)

            credit(4)
            s4 = q[4]
            W4 = CH * F1

            def bank_of(g):
                return pair[:, ds((g % 2) * 512, W4)]
            pe.wait_ge(q[3]["h_done"], T)
            M(bank_of(0), zb[:, 0:P], zb[:, 0:W4], start=True, stop=False)
            with pe.Fori(0, T) as t:
                def visit(g, v, new):
                    if new:
                        M(bank_of(g - 1), zb[:, 0:P], zb[:, 0:W4],
                          start=False, stop=True).then_inc(s4["rows_done"], 1)
                        pe.wait_ge(s4["pay_rdy"], g - 1)
                        M(bank_of(g), zb[:, 0:P], zb[:, 0:W4], start=True, stop=False)
                    pe.wait_ge(s4["same_rdy"], g * CH + 3 * CH)
                    pe.wait_ge(s4["pick_rdy"], v)
                    for k in range(CH):
                        pe.wait_ge(s4["oh_ready"], v * CH + (k + 1))
                        M(pick_ps[:, k * P:(k + 1) * P], oh[:, k, :],
                          same[:, ds(g % 2, 1), k * P:(k + 1) * P].rearrange("p o e -> p (o e)"),
                          start=True, stop=True).then_inc(s4["oh_free"], 1)
                    pe.wait_ge(s4["pick_rdy"], v + 1)
                    for k in range(CH):
                        M(pair[:, ds((g % 2) * 512 + k * F1, F1)], pick[:, k * P:(k + 1) * P],
                          h3[:, ds(t, 1), :].rearrange("p o c -> p (o c)"), start=False, stop=False)
                visits(pe, t, visit)
            M(bank_of(G - 1), zb[:, 0:P], zb[:, 0:W4], start=False, stop=True).then_inc(s4["rows_done"], 1)

            with pe.Fori(0, T // FB // 2) as i:
                for h in range(2):
                    m = i * 2 + h
                    pe.wait_ge(z_sum, m + 3)
                    for a in range(FB):
                        n = m * FB + a
                        par = (h * FB + a) % 2
                        nc.tensor.transpose(bank[3 + par][0:F1, 0:P], dsum[:, a * F1:(a + 1) * F1], ident[:, :]).then_inc(z_tp, 1)
                        pe.wait_ge(z_cp, n + 1)
                        if a >= 2:
                            pe.wait_ge(z_out, n - 1)
                        M(bank[5 + par][:, 0:F], aT[par][:, :], w3s[:, :], start=True, stop=True).then_inc(z_mm, 1)


def kernel(**inputs):
    import concourse.bacc as bacc
    from concourse.bass_utils import run_bass_kernel_spmd

    a = {k: np.ascontiguousarray(v) for k, v in inputs.items()}
    f32 = np.float32
    x = np.zeros((T * P, F), f32)
    x[:N] = a["x"]
    dst = np.full(EPAD + 2, -1, np.int32)
    dst[1:1 + E] = a["dst"]
    src = np.zeros(G * GE, np.int32)
    src[:E] = a["src"]
    ea_t = np.zeros((F, EPAD), f32)
    ea_t[:, :E] = a["edge_attr_64"].T
    arrays = {
        "x": x.reshape(T, P, F).transpose(1, 0, 2),
        "dst_line": dst,
        "dst_cols": dst[1:1 + G * GE].reshape(G, P, CH).transpose(1, 0, 2).reshape(P, G * CH),
        "src_cols": src.reshape(G, P, CH).transpose(1, 0, 2).reshape(P, G * CH),
        "src_rows": src.reshape(G, P, CH).transpose(0, 2, 1).reshape(-1),
        "ea_t": ea_t,
        "w0": a["L0_gnn_W"],
        "w1": np.concatenate([a["L1_gnn_W1_l"].T, a["L1_gnn_W1_r"].T], 0),
        "b1": a["L1_gnn_b1"].reshape(HID, 1),
        "w2": np.concatenate([a["L1_gnn_W2_l"].T, a["L1_gnn_W2_r"].T], 1),
        "b2": a["L1_gnn_b2"],
        "wfcr": a["L2_gnn_W_fcr"].T,
        "wfc": a["L2_gnn_W_fc"].T,
        "loop_w": a["L2_gnn_loop_W"],
        "w3b": np.concatenate([a["L3_gnn_W"].T, a["L3_gnn_b"].reshape(1, F)], 0),
    }
    nc = bacc.Bacc("TRN2", target_bir_lowering=False, num_devices=1)
    args = {}
    for name, v in arrays.items():
        arrays[name] = np.ascontiguousarray(v)
        args[name] = nc.dram_tensor(f"in_{name}", v.shape, mybir.dt.from_np(v.dtype), kind="ExternalInput").ap()
    out = nc.dram_tensor("out", (P, T, F), mybir.dt.float32, kind="ExternalOutput").ap()
    gnn_kernel(nc, out=out, **args)
    r = run_bass_kernel_spmd(nc, [{f"in_{k}": v for k, v in arrays.items()}], core_ids=[0])
    return r.results[0]["out"].transpose(1, 0, 2).reshape(T * P, F)[:N]
```
